# Optimizing a Trainium2 kernel written in Bass

```python
import numpy as np
import jax
import jax.numpy as jnp

def _softmax(x, axis=-1):
    return jax.nn.softmax(x, axis=axis)

def _gelu(x):
    return jax.nn.gelu(x, approximate=True)

def _silu(x):
    return jax.nn.silu(x)

def _sigmoid(x):
    return jax.nn.sigmoid(x)

def _layernorm(x, axis=-1, eps=1e-05):
    m = jnp.mean(x, axis=axis, keepdims=True)
    v = jnp.var(x, axis=axis, keepdims=True)
    return (x - m) / jnp.sqrt(v + eps)

def _scatter_add(tgt, idx, src, axis=0):
    return tgt.at[idx].add(src)

def _segment_sum(src, seg, n):
    return jax.ops.segment_sum(src, seg, n)
kernel_name = 'mk_flamingo_gated_d1_seqx_r2_c312c7'

def setup_inputs(seed: int=0):
    np.random.seed(seed)
    _w = jnp.asarray

    def _rec_inputs():
        import jax
        import jax.numpy as jnp
        _rk = jax.random.key(seed)
        x = -0.0002928 + 1 * jax.random.normal(jax.random.fold_in(_rk, 1), (16, 224, 512), jnp.float32)
        _lenS = 224 - jax.random.randint(jax.random.fold_in(_rk, 7), (16,), 0, max(1, 224 // 4) + 1, jnp.int32)
        _lenS2 = 750 - jax.random.randint(jax.random.fold_in(_rk, 8), (16,), 0, max(1, 750 // 4) + 1, jnp.int32)
        _ctx_1024P = jax.random.normal(jax.random.fold_in(_rk, 11), (16, 16, 512), jnp.float32)
        _ctx_1024c = jax.random.dirichlet(jax.random.fold_in(_rk, 511), 0.3 * jnp.ones((16,), jnp.float32), (16, 750))
        _ctx_1024t = jnp.einsum('bsk,bkd->bsd', _ctx_1024c, _ctx_1024P)
        _ctx_1024t = _ctx_1024t * jax.lax.rsqrt(jnp.mean(jnp.square(_ctx_1024t)) + 1e-12) * 0.953939
        ctx_1024 = -1.39393e-06 + 0.999914 * (_ctx_1024t + 0.3 * jax.random.normal(jax.random.fold_in(_rk, 611), (16, 750, 512), jnp.float32))
        _g = jax.random.normal(jax.random.fold_in(_rk, 9001), (2, 1), jnp.float32)
        _g = jnp.sign(_g) * jnp.maximum(jnp.abs(_g), 1.0) + (_g == 0) * 1.0
        g_xattn = _g[0]
        g_ffn = _g[1]
        return (x, ctx_1024, g_xattn, g_ffn)
    x, ctx_1024, g_xattn, g_ffn = _rec_inputs()

    def _L0_xattn_setup():
        import jax, jax.numpy as jnp
        import numpy as np
        EMBED_DIM = 512
        NUM_HEADS = 16
        HEAD_DIM = EMBED_DIM // NUM_HEADS
        key = jax.random.key(seed)
        ks = jax.random.split(key, 7)
        B, S, E = (2, 1024, EMBED_DIM)
        bound = float(np.sqrt(6.0 / (E + E)))
        mkw = lambda k: jax.random.uniform(k, (E, E), jnp.float32, -bound, bound)
        return {'query': jax.random.normal(ks[0], (B, S, E), jnp.float32), 'key': jax.random.normal(ks[1], (B, S, E), jnp.float32), 'value': jax.random.normal(ks[2], (B, S, E), jnp.float32), 'Wq': mkw(ks[3]), 'Wk': mkw(ks[4]), 'Wv': mkw(ks[5]), 'Wo': mkw(ks[6])}
    _L0_xattn_all = _L0_xattn_setup()
    _L0_xattn_in = {k: v for k, v in _L0_xattn_all.items() if k in ('Wq', 'Wk', 'Wv', 'Wo')}
    del _L0_xattn_all

    def _L0_ffn_setup():
        import jax, jax.numpy as jnp
        import numpy as np
        NUM_EXPERTS = 8
        D_MODEL = 512
        D_FF = 2048
        BATCH, SEQ = (2, 2048)
        key = jax.random.key(seed)
        k_x, k_w1, k_w2 = jax.random.split(key, 3)
        x = jax.random.normal(k_x, (BATCH, SEQ, D_MODEL), dtype=jnp.float32)
        w1 = jax.random.normal(k_w1, (NUM_EXPERTS, D_MODEL, D_FF), dtype=jnp.float32) * (1.0 / np.sqrt(D_MODEL))
        b1 = jnp.zeros((NUM_EXPERTS, D_FF), dtype=jnp.float32)
        w2 = jax.random.normal(k_w2, (NUM_EXPERTS, D_FF, D_MODEL), dtype=jnp.float32) * (1.0 / np.sqrt(D_FF))
        b2 = jnp.zeros((NUM_EXPERTS, D_MODEL), dtype=jnp.float32)
        return {'x': x, 'w1': w1, 'b1': b1, 'w2': w2, 'b2': b2}
    _L0_ffn_all = _L0_ffn_setup()
    _L0_ffn_in = {k: v for k, v in _L0_ffn_all.items() if k in ('w1', 'b1', 'w2', 'b2')}
    del _L0_ffn_all
    return {'x': x, 'ctx_1024': ctx_1024, 'g_xattn': g_xattn, 'g_ffn': g_ffn, 'L0_xattn_Wq': _L0_xattn_in['Wq'], 'L0_xattn_Wk': _L0_xattn_in['Wk'], 'L0_xattn_Wv': _L0_xattn_in['Wv'], 'L0_xattn_Wo': _L0_xattn_in['Wo'], 'L0_ffn_w1': _L0_ffn_in['w1'], 'L0_ffn_b1': _L0_ffn_in['b1'], 'L0_ffn_w2': _L0_ffn_in['w2'], 'L0_ffn_b2': _L0_ffn_in['b2']}

def reference(x, ctx_1024, g_xattn, g_ffn, L0_xattn_Wq, L0_xattn_Wk, L0_xattn_Wv, L0_xattn_Wo, L0_ffn_w1, L0_ffn_b1, L0_ffn_w2, L0_ffn_b2):
    import jax
    import jax.numpy as jnp

    def _L0_xattn_ref(query, key, value, Wq, Wk, Wv, Wo):
        import jax, jax.numpy as jnp
        import numpy as np
        EMBED_DIM = 512
        NUM_HEADS = 16
        HEAD_DIM = EMBED_DIM // NUM_HEADS
        B, L, E = query.shape
        H, D = (NUM_HEADS, HEAD_DIM)
        scale = D ** (-0.5)
        q = (query @ Wq.T).reshape(B, L, H, D) * scale
        k = (key @ Wk.T).reshape(B, -1, H, D)
        v = (value @ Wv.T).reshape(B, -1, H, D)
        scores = jax.nn.sigmoid(jnp.einsum('blhd,bshd->bhls', q, k))
        o = jnp.einsum('bhls,bshd->blhd', scores, v).reshape(B, L, E)
        return o @ Wo.T

    def _L0_ffn_ref(x, w1, b1, w2, b2):
        import jax, jax.numpy as jnp
        import numpy as np
        NUM_EXPERTS = 8
        D_MODEL = 512
        D_FF = 2048
        BATCH, SEQ = (2, 2048)
        B, S, D = x.shape
        E = w1.shape[0]
        T = B * S // E
        tokens = x.reshape(E, T, D)
        h = jnp.einsum('etd,edf->etf', tokens, w1) + b1[:, None, :]
        h = jax.nn.gelu(h)
        y = jnp.einsum('etf,efd->etd', h, w2) + b2[:, None, :]
        return y.reshape(B, S, D)
    x = x + jnp.tanh(g_xattn[0]) * _L0_xattn_ref(_layernorm(x, axis=-1), ctx_1024, ctx_1024, L0_xattn_Wq, L0_xattn_Wk, L0_xattn_Wv, L0_xattn_Wo)
    x = x + jnp.tanh(g_ffn[0]) * _L0_ffn_ref(_layernorm(x, axis=-1), L0_ffn_w1, L0_ffn_b1, L0_ffn_w2, L0_ffn_b2)
    return x

_drawn_inputs = setup_inputs


def setup_inputs(seed=0):
    import zlib

    import numpy as np

    out = dict(_drawn_inputs(seed))
    spreads = {'L0_ffn_b1': (0.0, 2.0), 'L0_ffn_b2': (0.0, 2.0)}
    factors = {'L0_ffn_w1': 8.0, 'L0_ffn_w2': 8.0}
    for name, (base, spread) in spreads.items():
        noise = np.random.default_rng([zlib.crc32(name.encode()), seed]).standard_normal(out[name].shape)
        drawn = base * np.exp(spread * noise) if base else spread * noise
        out[name] = jnp.asarray(drawn.astype(out[name].dtype))
    for name, factor in factors.items():
        out[name] = (out[name] * factor).astype(out[name].dtype)
    return out
```

```python
from contextlib import ExitStack

import concourse.bass as bass
from concourse import mybir

F32 = mybir.dt.float32
F32R = mybir.dt.float32r
I32 = mybir.dt.int32
ALU = mybir.AluOpType
ACT = mybir.ActivationFunctionType

P = 128
HI, LO = 0, 1
TERMS = ((HI, HI), (HI, LO), (LO, HI))
RSQRT_SEED = float(0x5F3759DF)
EPS = 1e-5


def rsqrt_steps(nc, y, v, tmp, var):
    yield lambda: nc.vector.tensor_scalar(v, var, EPS, None, ALU.add)
    yield lambda: nc.vector.tensor_scalar(y.bitcast(I32), v.bitcast(I32), -0.5, RSQRT_SEED, ALU.mult, ALU.add)
    for _ in range(3):
        yield lambda: nc.vector.scalar_tensor_tensor(out=tmp, in0=y, scalar=-0.5, in1=y, op0=ALU.mult, op1=ALU.mult)
        yield lambda: nc.vector.tensor_tensor(tmp, tmp, v, ALU.mult)
        yield lambda: nc.vector.scalar_tensor_tensor(out=y, in0=tmp, scalar=1.5, in1=y, op0=ALU.add, op1=ALU.mult)


LN_STEPS = 2 + 2 + 11


def attention(nc, io, scr):
    B, L, D = io["x"].shape
    S = io["ctxT"].shape[2]
    KT = D // P
    HEADS = 4
    HD = P // HEADS
    LT = L // 2
    SC = S // 3
    ST = S // 6
    STEPS = KT * 3
    SCALE = float(HD) ** -0.5
    assert L == 2 * LT and S == 6 * ST and LT <= P and ST <= P and 2 * L <= 512

    PREP, OUT = "TKVQ", "OU"
    FILL = [(0, "A", "T", 0), (0, "A", "T", 1), (0, "B", "K", 0),
            (1, "A", "K", 1), (1, "B", "O", 0), (2, "A", "K", 2), (2, "B", "O", 1),
            (3, "A", "K", 3), (3, "B", "V", 0), (4, "A", "K", 4), (4, "B", "V", 1),
            (5, "A", "K", 5), (5, "B", "Q", 0), (5, "B", "U", 0), (5, "B", "U", 1),
            (6, "A", "K", 6), (6, "B", "V", 2), (7, "A", "K", 7), (7, "B", "V", 3),
            (8, "A", "K", 8), (8, "B", "Q", 1), (8, "B", "Q", 2),
            (9, "A", "K", 9), (9, "B", "V", 4), (10, "A", "K", 10), (10, "B", "V", 5),
            (11, "A", "K", 11), (11, "B", "Q", 3)]
    BANK = {(k, i): g % 3 for g, (_, _, k, i) in enumerate(FILL)}
    BANK["T", 0], BANK["T", 1] = 1, 0
    COUNT = {"T": 2, "K": 12, "V": 6, "Q": 4, "O": 2, "U": 2}

    def present(prep, out):
        return [(s, a, k, i) for s, a, k, i in FILL if (k in PREP and prep) or (k in OUT and out)]

    with ExitStack() as ctx:
        def sb(name, shape, dt=F32):
            return ctx.enter_context(nc.sbuf_tensor(name, shape, dt))

        def sem(name):
            return ctx.enter_context(nc.semaphore(name))

        scores_ps = ctx.enter_context(nc.psum_tensor("scores_ps", [P, HEADS, 512], F32))
        heads_ps = ctx.enter_context(nc.psum_tensor("heads_ps", [P, 512], F32))
        fill_ps = ctx.enter_context(nc.psum_tensor("fill_ps", [P, 3, 512], F32))

        w = {k: sb(f"w{k}", [P, 2, KT, D], F32R) for k in "KQVO"}
        ctx_raw = sb("ctx_raw", [P, KT, SC])
        ctx_hl = sb("ctx_hl", [P, 3, 2, KT, SC], F32R)
        k_stage = sb("k_stage", [P, 2, 2, SC], F32R)
        q_stage = sb("q_stage", [P, 2, 2, L], F32R)
        v_stage = sb("v_stage", [ST, 2, D])
        k_st3 = sb("k_st3", [3 * HD, 2, HEADS, S], F32R)
        q_st3 = sb("q_st3", [3 * HD, 2, HEADS, L], F32R)
        v_sb = sb("v_sb", [ST, 2, 6, P])
        probs = sb("probs", [P, 2, HEADS, 2 * L])
        x_ln = sb("x_ln", [LT, 2, D])
        x_res = sb("x_res", [LT, 2, D])
        x1 = sb("x1", [LT, 2, D])
        x1n = sb("x1n", [LT, 2, D])
        xnT = sb("xnT", [P, 2, KT, L], F32R)
        oT = sb("oT", [P, 2, KT, L], F32R)
        x1nT = sb("x1nT", [P, KT, L])
        ident = sb("ident", [P, P])
        g_in = sb("g_in", [P, 1])
        gate = sb("gate", [P, 1])
        stats = sb("stats", [LT, 2, 2, 6])
        mv = sb("mv", [LT, 2, 2, 2])
        rstd = sb("rstd", [LT, 2, 2])
        nv = sb("nv", [LT, 2, 2])
        ntmp = sb("ntmp", [LT, 2, 2])

        w_raw = probs[:, :, :, :].rearrange("p a h l -> p (a h l)")
        WR = 3
        HALF = (KT // 2) * D

        s_w_in = [sem(f"w_in{r}") for r in range(WR)]
        s_w_hi, s_w_lo = sem("w_hi"), sem("w_lo")
        s_ctx_in, s_ctx_hi, s_ctx_lo = sem("ctx_in"), sem("ctx_hi"), sem("ctx_lo")
        s_x_in, s_xr_in, s_g_in, s_gate = sem("x_in"), sem("xr_in"), sem("g_in_s"), sem("gate_s")
        s_ident = sem("ident_s")
        s_xn = sem("xn_ready")
        s_x1, s_x1n = sem("x1_ready"), sem("x1n_ready")
        s_ln = [sem("ln_x_step"), sem("ln_x1_step")]
        full = {k: sem(f"full_{k}") for k in "TKVQOU"}
        hi = {k: sem(f"hi_{k}") for k in "TKQ"}
        done = {k: sem(f"done_{k}") for k in "TKVQU"}
        done["O"] = s_x1
        s_kq_in = [sem(f"kq_in{r}") for r in range(2)]
        s_v_in = [sem(f"v_in{r}") for r in range(2)]
        s_scores, s_probs, s_av = sem("scores_full"), sem("probs_ready"), sem("av_done")
        s_o_hi, s_o_lo = sem("oT_hi"), sem("oT_lo")
        s_k_st = [sem(f"k_stored{r}") for r in range(2)]
        s_q_st = [sem(f"q_stored{r}") for r in range(2)]
        s_v_st = [sem(f"v_stored{r}") for r in range(2)]
        s_x1_st, s_x1nT_st = sem("x1_stored"), sem("x1nT_stored")

        block = ctx.enter_context(nc.Block())

        def own(eng):
            eng.nop(nofuse=True)

        def batches(eng, body):
            body(-1, True, False, True)
            body(0, True, False, True)
            body(1, True, True, True)
            with eng.Fori(2, B - 2) as b:
                body(b, True, True, True)
            body(B - 2, True, True, False)
            body(B - 1, False, True, False)
            body(B, False, True, False)

        def attends(b):
            return not isinstance(b, int) or 0 <= b < B

        def known(b, value):
            return isinstance(b, int) and b == value

        def nth(kind, b, i):
            return COUNT[kind] * (b + 1 if kind in PREP else b - 1) + i + 1

        def at(eng, sem_, value):
            if not isinstance(value, int) or value > 0:
                eng.wait_ge(sem_, value)

        def alone(eng, sem_, value):
            at(eng, sem_, value)
            own(eng)

        def bank_free(pe, b, prep, out, kind, i):
            todo = [(k, j) for _, _, k, j in present(prep, out)]
            mine = todo.index((kind, i))
            before = [g for g in todo[:mine] if BANK[g] == BANK[kind, i]]
            if before:
                k, j = before[-1]
                pe.wait_ge(done[k], nth(k, b, j))
                return
            if isinstance(b, int) and b < 0:
                return
            if isinstance(b, int):
                last = present(b - 1 < B - 1, b - 1 > 0)
            else:
                last = present(True, True)
            last = [(k, j) for _, _, k, j in last if BANK[k, j] == BANK[kind, i]]
            if last:
                k, j = last[-1]
                pe.wait_ge(done[k], nth(k, b - 1, j))

        @block.sync
        def _(sp):
            def load_ctx(n, c):
                alone(sp, s_ctx_lo, 3 * n + c)
                sp.dma_start(ctx_raw[:], io["ctxT"][bass.ds(n, 1), :, c * SC:(c + 1) * SC]
                             .rearrange("a (t p) s -> p (a t) s", p=P)).then_inc(s_ctx_in, 16)

            def load_x(dst, b, s):
                sp.dma_start(dst[:], io["x"][bass.ds(b, 1)].rearrange("a (t p) d -> p (a t) d", p=LT)).then_inc(s, 16)

            def load_kq(b, mt, kq_b):
                slot = mt % 2
                alone(sp, s_scores, STEPS * kq_b + 3 * ((mt - 2) % KT) + 3)
                alone(sp, s_k_st[slot], 16 * (6 * b + (8 + mt) // 2 + 1))
                alone(sp, s_q_st[slot], 16 * (2 * b + mt // 2 + 1))
                for t, (kh, qh) in enumerate(((HI, HI), (LO, HI), (HI, LO))):
                    for dst, src, h in ((k_st3, scr["k"], kh), (q_st3, scr["q"], qh)):
                        sp.dma_start(dst[t * HD:(t + 1) * HD, slot].bitcast(F32),
                                     src[bass.ds(b, 1), h, mt * P:(mt + 1) * P, :]
                                     .rearrange("a (j p) s -> p (a j) s", p=HD)).then_inc(s_kq_in[slot], 16)

            def load_v(b, mt, v_b):
                slot = mt % 2
                alone(sp, s_av, STEPS * v_b + 3 * ((mt - 2) % KT) + 3)
                for r in range(2):
                    alone(sp, s_v_st[r], 16 * 3 * (b + 1))
                sp.dma_start(v_sb[:, slot], scr["v"][bass.ds(b, 1), :, mt * P:(mt + 1) * P]
                             .rearrange("a (t p) d -> p (a t) d", p=ST)).then_inc(s_v_in[slot], 16)

            def load_w(n):
                kind, half = "KQVO"[n // 2], n % 2
                r = n % WR
                alone(sp, s_w_lo, n - WR + 1)
                sp.dma_start(w_raw[:, r * HALF:(r + 1) * HALF].rearrange("p (t d) -> p t d", d=D),
                             io[f"W{kind}T"].rearrange("(t p) d -> p t d", p=P)[:, half * KT // 2:(half + 1) * KT // 2]
                             ).then_inc(s_w_in[r], 16)

            load_w(0)
            load_w(1)
            load_ctx(0, 0)
            load_x(x_ln, 0, s_x_in)
            sp.dma_start(g_in[:], io["g_xattn"].partition_broadcast(P)).then_inc(s_g_in, 16)
            for n in range(2, 8):
                load_w(n)

            def body(b, prep, out, ahead):
                here = attends(b)
                if prep:
                    load_ctx(b + 1, 1)
                if here:
                    load_v(b, 1, b - 1)
                if prep:
                    load_ctx(b + 1, 2)
                if here:
                    load_kq(b, 2, b)
                    alone(sp, s_x1, 2 * b)
                    load_x(x_res, b, s_xr_in)
                if ahead:
                    alone(sp, full["T"], nth("T", b, 1))
                    load_x(x_ln, b + 2, s_x_in)
                if here:
                    load_v(b, 2, b)
                if ahead:
                    load_ctx(b + 2, 0)
                if here:
                    load_kq(b, 3, b)
                    load_v(b, 3, b)
                if prep:
                    load_kq(b + 1, 0, b)
                    load_v(b + 1, 0, b)
                    load_kq(b + 1, 1, b)

            batches(sp, body)

        @block.gpsimd
        def _(pool):
            nc.gpsimd.memset(ident[:], 0.0).then_inc(s_ident, 1)
            pool.wait_ge(s_ident, 1)
            nc.gpsimd.affine_select(out=ident[:], in_=ident[:], compare_op=ALU.not_equal, fill=1.0, base=0,
                                    pattern=[[-1, P]], channel_multiplier=1).then_inc(s_ident, 1)

            def body(b, prep, out, ahead):
                n = b + 1
                for _, _, kind, i in present(prep, out):
                    if kind in "KVQ":
                        alone(pool, done[kind], nth(kind, b, i))
                    if kind == "K":
                        c, mt = i // KT, i % KT
                        pool.dma_start(scr["k"][bass.ds(n, 1), :, mt * P:(mt + 1) * P, c * SC:(c + 1) * SC]
                                       .rearrange("a h p s -> p (a h) s"), k_stage[:, i % 2].bitcast(F32)).then_inc(s_k_st[i % 2], 16)
                    if kind == "Q":
                        pool.dma_start(scr["q"][bass.ds(n, 1), :, i * P:(i + 1) * P, :]
                                       .rearrange("a h p s -> p (a h) s"), q_stage[:, i % 2].bitcast(F32)).then_inc(s_q_st[i % 2], 16)
                    if kind == "V":
                        pool.dma_start(scr["v"][bass.ds(n, 1), i * ST:(i + 1) * ST, :]
                                       .rearrange("a p d -> p (a d)"), v_stage[:, i % 2]).then_inc(s_v_st[i % 2], 16)
                    if (kind, i) == ("O", 1):
                        alone(pool, s_x1, 2 * b)
                        pool.dma_start(scr["x1"][bass.ds(b - 1, 1)].rearrange("a (t p) d -> p (a t) d", p=LT),
                                       x1[:]).then_inc(s_x1_st, 16)
                    if (kind, i) == ("U", 1):
                        alone(pool, done["U"], 2 * b)
                        pool.dma_start(scr["x1nT"][bass.ds(b - 1, 1)].rearrange("a (t p) l -> p (a t) l", p=P),
                                       x1nT[:]).then_inc(s_x1nT_st, 16)

            batches(pool, body)
            pool.wait_ge(s_x1_st, 16 * B)
            pool.wait_ge(s_x1nT_st, 16 * B)
            for r in range(2):
                pool.wait_ge(s_k_st[r], 16 * 6 * B)
                pool.wait_ge(s_q_st[r], 16 * 2 * B)
                pool.wait_ge(s_v_st[r], 16 * 3 * B)

        @block.tensor
        def _(pe):
            def three_terms(out, lhsT, rhs):
                for kt in range(KT):
                    for t, (a, c) in enumerate(TERMS):
                        last = pe.matmul(out, lhsT(kt, a), rhs(kt, c), start=(kt == 0 and t == 0),
                                         stop=(kt == KT - 1 and t == 2))
                return last

            def scores(b, s):
                mt, pair = s // 3, s % 3
                slot = mt % 2
                if pair == 0:
                    pe.wait_ge(s_kq_in[slot], 16 * 6 * (2 * b + mt // 2 + 1))
                at(pe, s_probs, STEPS * b + s)
                for t in range(2):
                    for j in range(HEADS):
                        st = 2 * pair + t
                        last = pe.matmul(scores_ps[0:ST, j, t * L:(t + 1) * L],
                                         k_st3[:, slot, j, st * ST:(st + 1) * ST], q_st3[:, slot, j, :],
                                         start=True, stop=True)
                last.then_inc(s_scores, 1)

            def heads(b, s):
                mt, pair = s // 3, s % 3
                slot = mt % 2
                if pair == 0:
                    pe.wait_ge(s_v_in[slot], 16 * (2 * b + mt // 2 + 1))
                    at(pe, s_o_lo, KT * b + mt)
                pe.wait_ge(s_probs, STEPS * b + s + 1)
                for t in range(2):
                    for j in range(HEADS):
                        last = pe.matmul(heads_ps[j * HD:(j + 1) * HD, 0:L],
                                         v_sb[:, slot, 2 * pair + t, j * HD:(j + 1) * HD],
                                         probs[0:ST, s % 2, j, t * L:(t + 1) * L],
                                         start=(pair == 0 and t == 0), stop=(pair == 2 and t == 1))
                last.then_inc(s_av, 1)

            def fill(b, prep, out, kind, i):
                bank_free(pe, b, prep, out, kind, i)
                ps = fill_ps[:, BANK[kind, i], :]
                n = b + 1
                if kind == "T":
                    if i == 0:
                        pe.wait_ge(s_xn, n + 1)
                    for kt in range(KT):
                        last = pe.transpose(ps[:, kt * LT:(kt + 1) * LT], x_ln[:, i, kt * P:(kt + 1) * P], ident[0:LT, 0:LT])
                elif kind == "K":
                    c, mt = i // KT, i % KT
                    if mt == 0:
                        pe.wait_ge(s_ctx_lo, 3 * n + c + 1)
                    if known(n, 0) and i == 0:
                        pe.wait_ge(s_w_lo, 2)
                    last = three_terms(ps[:, 0:SC], lambda kt, a: w["K"][:, a, kt, mt * P:(mt + 1) * P],
                                       lambda kt, a: ctx_hl[:, c, a, kt, :])
                elif kind == "V":
                    c, r = i // 2, i % 2
                    if known(n, 0) and i == 0:
                        pe.wait_ge(s_w_lo, 8)
                    last = three_terms(ps[0:ST, :], lambda kt, a: ctx_hl[:, c, a, kt, r * ST:(r + 1) * ST],
                                       lambda kt, a: w["V"][:, a, kt, :])
                elif kind == "Q":
                    if i == 0:
                        pe.wait_ge(done["T"], nth("T", b, 1))
                    if known(n, 0) and i == 0:
                        pe.wait_ge(s_w_lo, 4)
                    last = three_terms(ps[:, 0:L], lambda kt, a: w["Q"][:, a, kt, i * P:(i + 1) * P],
                                       lambda kt, a: xnT[:, a, kt, :])
                elif kind == "O":
                    if i == 0:
                        pe.wait_ge(s_o_lo, KT * b)
                    last = three_terms(ps[0:LT, :], lambda kt, a: oT[:, a, kt, i * LT:(i + 1) * LT],
                                       lambda kt, a: w["O"][:, a, kt, :])
                else:
                    if i == 0:
                        pe.wait_ge(s_x1n, b)
                    for kt in range(KT):
                        last = pe.transpose(ps[:, kt * LT:(kt + 1) * LT], x1n[:, i, kt * P:(kt + 1) * P], ident[0:LT, 0:LT])
                last.then_inc(full[kind], 1)

            def body(b, prep, out, ahead):
                for s in range(STEPS):
                    if attends(b):
                        scores(b, s)
                    for _, _, kind, i in [f for f in present(prep, out) if f[0:2] == (s, "A")]:
                        fill(b, prep, out, kind, i)
                    if s == 0 and (not isinstance(b, int) or b > 0):
                        heads(b - 1, STEPS - 1)
                    if s > 0 and attends(b):
                        heads(b, s - 1)
                    for _, _, kind, i in [f for f in present(prep, out) if f[0:2] == (s, "B")]:
                        fill(b, prep, out, kind, i)

            pe.wait_ge(s_ident, 2)
            batches(pe, body)

        def split_points(s):
            return {1: (1, 1), 4: (1, 2), 8: (2, 0)}.get(s)

        @block.scalar
        def _(act):
            def ctx_hi(n, c):
                act.wait_ge(s_ctx_in, 16 * (3 * n + c + 1))
                at(act, full["K"], 12 * (n - 1) + KT * (c + 1))
                at(act, full["V"], 6 * (n - 1) + 2 * (c + 1))
                nc.scalar.copy(ctx_hl[:, c, HI], ctx_raw[:]).then_inc(s_ctx_hi, 1)

            def w_hi(n):
                act.wait_ge(s_w_in[n % WR], 16 * (n // WR + 1))
                nc.scalar.copy(w["KQVO"[n // 2]][:, HI, (n % 2) * KT // 2:(n % 2 + 1) * KT // 2, :],
                               w_raw[:, (n % WR) * HALF:(n % WR + 1) * HALF].rearrange("p (t d) -> p t d", d=D)
                               ).then_inc(s_w_hi, 1)

            def sigmoid(b, s):
                act.wait_ge(s_scores, STEPS * b + s + 1)
                at(act, s_av, STEPS * b + s - 1)
                if known(b, 0) and s == 0:
                    act.wait_ge(s_w_lo, 8)
                nc.scalar.activation(probs[0:ST, s % 2], scores_ps[0:ST, :, 0:2 * L], ACT.Sigmoid,
                                     scale=SCALE).then_inc(s_probs, 1)

            def o_hi(b, mt):
                act.wait_ge(s_av, STEPS * b + 3 * mt + 3)
                if mt == 0:
                    at(act, full["O"], 2 * b)
                nc.scalar.copy(oT[:, HI, mt, :], heads_ps[:, 0:L]).then_inc(s_o_hi, 1)

            def leave(b, kind, i):
                n = b + 1
                if kind == "O":
                    return
                act.wait_ge(full[kind], nth(kind, b, i))
                ps = fill_ps[:, BANK[kind, i], :]
                if kind == "T":
                    if i == 0:
                        at(act, full["Q"], 4 * n)
                    nc.scalar.copy(xnT[:, HI, :, i * LT:(i + 1) * LT],
                                   ps[:, 0:KT * LT].rearrange("p (t l) -> p t l", l=LT)).then_inc(hi["T"], 1)
                elif kind == "K":
                    at(act, s_k_st[i % 2], 16 * (6 * n + i // 2))
                    nc.scalar.copy(k_stage[:, i % 2, HI, :], ps[:, 0:SC]).then_inc(hi["K"], 1)
                elif kind == "Q":
                    at(act, s_q_st[i % 2], 16 * (2 * n + i // 2))
                    nc.scalar.copy(q_stage[:, i % 2, HI, :], ps[:, 0:L]).then_inc(hi["Q"], 1)
                elif kind == "V":
                    at(act, s_v_st[i % 2], 16 * (3 * n + i // 2))
                    nc.scalar.copy(v_stage[:, i % 2, :], ps[0:ST, :]).then_inc(done["V"], 1)
                else:
                    if i == 0:
                        at(act, s_x1nT_st, 16 * (b - 1))
                    nc.scalar.copy(x1nT[:, :, i * LT:(i + 1) * LT],
                                   ps[:, 0:KT * LT].rearrange("p (t l) -> p t l", l=LT)).then_inc(done["U"], 1)

            w_hi(0)
            w_hi(1)
            ctx_hi(0, 0)
            for n in range(2, 8):
                w_hi(n)
            act.wait_ge(s_g_in, 16)
            nc.scalar.activation(gate[:], g_in[:], ACT.Tanh).then_inc(s_gate, 1)

            def body(b, prep, out, ahead):
                for s in range(STEPS):
                    if attends(b):
                        sigmoid(b, s)
                    for _, _, kind, i in [f for f in present(prep, out) if f[0:2] == (s, "A")]:
                        leave(b, kind, i)
                    if s == 0 and (not isinstance(b, int) or b > 0):
                        o_hi(b - 1, KT - 1)
                    if s > 0 and s % 3 == 0 and attends(b):
                        o_hi(b, s // 3 - 1)
                    for _, _, kind, i in [f for f in present(prep, out) if f[0:2] == (s, "B")]:
                        leave(b, kind, i)
                    split = split_points(s)
                    if split and (prep if split[0] == 1 else ahead):
                        ctx_hi(b + split[0], split[1])

            batches(act, body)

        @block.vector
        def _(dve):
            def ctx_lo(n, c):
                dve.wait_ge(s_ctx_hi, 3 * n + c + 1)
                nc.vector.tensor_tensor(ctx_hl[:, c, LO], ctx_raw[:], ctx_hl[:, c, HI].bitcast(F32),
                                        ALU.subtract).then_inc(s_ctx_lo, 1)

            def w_lo(n):
                dve.wait_ge(s_w_hi, n + 1)
                part = w["KQVO"[n // 2]][:, :, (n % 2) * KT // 2:(n % 2 + 1) * KT // 2, :]
                nc.vector.tensor_tensor(part[:, LO],
                                        w_raw[:, (n % WR) * HALF:(n % WR + 1) * HALF].rearrange("p (t d) -> p t d", d=D),
                                        part[:, HI].bitcast(F32), ALU.subtract).then_inc(s_w_lo, 1)

            def layernorm(which, n, src, dst, ready):
                steps = [lambda t=t: nc.vector.bn_stats(stats[:, which, t, :], src[:, t, :]) for t in range(2)]
                steps += [lambda t=t: nc.vector.bn_aggr(mv[:, which, t, :], stats[:, which, t, :]) for t in range(2)]
                steps += list(rsqrt_steps(nc, rstd[:, which, :], nv[:, which, :], ntmp[:, which, :], mv[:, which, :, 1]))
                for i, step in enumerate(steps):
                    if i in (2, 3):
                        own(dve)
                    step().then_inc(s_ln[which], 1)
                    dve.wait_ge(s_ln[which], LN_STEPS * n + i + 1)
                for t in range(2):
                    last = nc.vector.tensor_scalar(dst[:, t, :], src[:, t, :], mv[:, which, t, 0:1],
                                                   rstd[:, which, t:t + 1], ALU.subtract, ALU.mult)
                last.then_inc(ready, 1)

            def ln_x(n):
                dve.wait_ge(s_x_in, 16 * (n + 1))
                layernorm(0, n, x_ln, x_ln, s_xn)

            def ln_x1(b):
                dve.wait_ge(s_x1, 2 * b)
                at(dve, full["U"], 2 * (b - 1))
                layernorm(1, b - 1, x1, x1n, s_x1n)

            def o_lo(b, mt):
                dve.wait_ge(s_o_hi, KT * b + mt + 1)
                nc.vector.tensor_tensor(oT[:, LO, mt, :], heads_ps[:, 0:L], oT[:, HI, mt, :].bitcast(F32),
                                        ALU.subtract).then_inc(s_o_lo, 1)

            def leave(b, kind, i):
                ps = fill_ps[:, BANK[kind, i], :]
                if kind in "TKQ":
                    dve.wait_ge(hi[kind], nth(kind, b, i))
                if kind == "T":
                    nc.vector.tensor_tensor(xnT[:, LO, :, i * LT:(i + 1) * LT],
                                            ps[:, 0:KT * LT].rearrange("p (t l) -> p t l", l=LT),
                                            xnT[:, HI, :, i * LT:(i + 1) * LT].bitcast(F32),
                                            ALU.subtract).then_inc(done["T"], 1)
                elif kind == "K":
                    nc.vector.tensor_tensor(k_stage[:, i % 2, LO, :], ps[:, 0:SC], k_stage[:, i % 2, HI, :].bitcast(F32),
                                            ALU.subtract).then_inc(done["K"], 1)
                elif kind == "Q":
                    nc.vector.tensor_tensor(q_stage[:, i % 2, LO, :], ps[:, 0:L], q_stage[:, i % 2, HI, :].bitcast(F32),
                                            ALU.subtract).then_inc(done["Q"], 1)
                elif kind == "O":
                    dve.wait_ge(full["O"], nth("O", b, i))
                    if i == 0:
                        dve.wait_ge(s_xr_in, 16 * b)
                        at(dve, s_x1_st, 16 * (b - 1))
                    nc.vector.scalar_tensor_tensor(out=x1[:, i, :], in0=ps[0:LT, :], scalar=gate[0:LT, 0:1],
                                                   in1=x_res[:, i, :], op0=ALU.mult, op1=ALU.add).then_inc(s_x1, 1)

            w_lo(0)
            w_lo(1)
            ctx_lo(0, 0)
            ln_x(0)
            for n in range(2, 8):
                w_lo(n)
            dve.wait_ge(s_gate, 1)

            def body(b, prep, out, ahead):
                for s in range(STEPS):
                    for _, _, kind, i in [f for f in present(prep, out) if f[0:2] == (s, "A")]:
                        leave(b, kind, i)
                    if s == 0 and (not isinstance(b, int) or b > 0):
                        o_lo(b - 1, KT - 1)
                    if s > 0 and s % 3 == 0 and attends(b):
                        o_lo(b, s // 3 - 1)
                    for _, _, kind, i in [f for f in present(prep, out) if f[0:2] == (s, "B")]:
                        leave(b, kind, i)
                    split = split_points(s)
                    if split and (prep if split[0] == 1 else ahead):
                        ctx_lo(b + split[0], split[1])
                    if s == 3 and out:
                        ln_x1(b)
                    if s == 6 and ahead:
                        ln_x(b + 2)

            batches(dve, body)


def feed_forward(nc, io, scr, out):
    E, D, F = io["w1"].shape
    B, L, _ = io["x"].shape
    KT = D // P
    T = B * L // E
    TT = T // 4
    FC = 2 * P
    C = F // FC
    NB = T // L
    assert T == NB * L and TT <= P and T <= 512 and C % 2 == 0

    with ExitStack() as ctx:
        def sb(name, shape, dt=F32):
            return ctx.enter_context(nc.sbuf_tensor(name, shape, dt))

        def sem(name):
            return ctx.enter_context(nc.semaphore(name))

        hid_ps = ctx.enter_context(nc.psum_tensor("hid_ps", [P, 2, 512], F32))
        y_ps = ctx.enter_context(nc.psum_tensor("y_ps", [P, KT, 512], F32))
        turn_ps = ctx.enter_context(nc.psum_tensor("turn_ps", [P, 2, 512], F32))

        w1_raw = sb("w1_raw", [P, 2, KT, FC])
        w2_raw = sb("w2_raw", [P, 2, 2, D])
        w1 = sb("w1_hl", [P, 2, 2, KT, FC], F32R)
        w2 = sb("w2_hl", [P, 2, 2, 2, D], F32R)
        xt_raw = sb("xt_raw", [P, KT, NB, L])
        xt = sb("xt_hl", [P, 2, KT, NB, L], F32R)
        hid = sb("hid", [P, 2, T])
        hid_hl = sb("hid_hl", [P, 2, 2, 2, T], F32R)
        yT = sb("yT", [P, KT, T])
        res = sb("res", [TT, 4, D])
        o = sb("o_sb", [TT, 4, D])
        b1 = sb("b1_sb", [P, 2 * C])
        b2 = sb("b2_sb", [P, KT])
        ident = sb("ident2", [P, P])
        g_in = sb("g2_in", [P, 1])
        gate = sb("gate2", [P, 1])

        s_w_in = {(m, r): sem(f"w{m}_in{r}") for m in (1, 2) for r in range(2)}
        s_w_hi = {m: sem(f"w{m}_hi_s") for m in (1, 2)}
        s_w_lo = {m: sem(f"w{m}_lo_s") for m in (1, 2)}
        s_xt_in, s_xt_hi, s_xt_lo = sem("xt_in"), sem("xt_hi_s"), sem("xt_lo_s")
        s_b1_in, s_b2_in, s_res_in, s_g_in, s_gate, s_ident = sem("b1_in_s"), sem("b2_in_s"), sem("res_in"), sem("g2_in_s"), sem("gate2_s"), sem("ident2_s")
        s_hid_full, s_gelu, s_h_hi, s_h_lo = sem("hid_full"), sem("gelu_ready"), sem("hid_hi"), sem("hid_lo")
        s_y_chunk, s_yT, s_turned, s_out, s_stored = sem("y_chunk"), sem("yT_ready"), sem("turned"), sem("out_ready"), sem("out_stored")

        block = ctx.enter_context(nc.Block())

        def own(eng):
            eng.nop(nofuse=True)

        def experts(eng, body):
            body(0, False)
            body(1, True)
            with eng.Fori(2, E) as e:
                body(e, True)

        def at(eng, sem_, value):
            if not isinstance(value, int) or value > 0:
                eng.wait_ge(sem_, value)

        def alone(eng, sem_, value):
            at(eng, sem_, value)
            own(eng)

        @block.sync
        def _(sp):
            sp.dma_start(g_in[:], io["g_ffn"].partition_broadcast(P)).then_inc(s_g_in, 16)

            def body(e, _):
                alone(sp, s_xt_lo, e)
                for i in range(NB):
                    sp.dma_start(xt_raw[:, :, i, :], scr["x1nT"][bass.ds(e * NB + i, 1)].rearrange("b (t p) l -> p (b t) l", p=P)
                                 ).then_inc(s_xt_in, 16)
                for c in range(C):
                    slot = c % 2
                    alone(sp, s_w_lo[1], C * e + c - 1)
                    sp.dma_start(w1_raw[:, slot], io["w1"][bass.ds(e, 1), :, c * FC:(c + 1) * FC]
                                 .rearrange("a (t p) f -> p (a t) f", p=P)).then_inc(s_w_in[1, slot], 16)
                    if c == 0:
                        alone(sp, s_gelu, 2 * C * e)
                        sp.dma_start(b1[:], io["b1"][bass.ds(e, 1)].rearrange("a p f -> p (a f)")).then_inc(s_b1_in, 16)
                    if c == 2:
                        alone(sp, s_yT, KT * e)
                        sp.dma_start(b2[:], io["b2"][bass.ds(e, 1)].rearrange("a p f -> p (a f)")).then_inc(s_b2_in, 16)
                    alone(sp, s_w_lo[2], C * e + c - 1)
                    sp.dma_start(w2_raw[:, slot], io["w2"][bass.ds(e, 1), c * FC:(c + 1) * FC, :]
                                 .rearrange("a (t p) d -> p (a t) d", p=P)).then_inc(s_w_in[2, slot], 16)
                    if c == 3:
                        alone(sp, s_out, 4 * e)
                        sp.dma_start(res[:], scr["x1"][bass.ds(e * NB, NB)].rearrange("b (t p) d -> p (b t) d", p=TT)
                                     ).then_inc(s_res_in, 16)

            experts(sp, body)

        @block.gpsimd
        def _(pool):
            nc.gpsimd.memset(ident[:], 0.0).then_inc(s_ident, 1)
            pool.wait_ge(s_ident, 1)
            nc.gpsimd.affine_select(out=ident[:], in_=ident[:], compare_op=ALU.not_equal, fill=1.0, base=0,
                                    pattern=[[-1, P]], channel_multiplier=1).then_inc(s_ident, 1)

            def store(e):
                alone(pool, s_out, 4 * e + 4)
                pool.dma_start(out[bass.ds(e * NB, NB)].rearrange("b (t p) d -> p (b t) d", p=TT), o[:]
                               ).then_inc(s_stored, 16)

            with pool.Fori(0, E) as e:
                store(e)
            pool.wait_ge(s_stored, 16 * E)

        @block.tensor
        def _(pe):
            def hidden(e, c, k):
                slot = c % 2
                if k == 0:
                    pe.wait_ge(s_w_lo[1], C * e + c + 1)
                    if c == 0:
                        pe.wait_ge(s_xt_lo, e + 1)
                at(pe, s_gelu, 2 * (C * e + c - 1) + k + 1)
                for kt in range(KT):
                    for t, (a, d) in enumerate(TERMS):
                        last = pe.matmul(hid_ps[:, k, 0:T], w1[:, slot, a, kt, k * P:(k + 1) * P],
                                         xt[:, d, kt].rearrange("p b l -> p (b l)"),
                                         start=(kt == 0 and t == 0), stop=(kt == KT - 1 and t == 2))
                last.then_inc(s_hid_full, 1)

            def y(e, c):
                slot = c % 2
                pe.wait_ge(s_w_lo[2], C * e + c + 1)
                pe.wait_ge(s_h_lo, C * e + c + 1)
                if c == 0:
                    at(pe, s_yT, KT * e)
                for dt in range(KT):
                    for k in range(2):
                        for t, (a, d) in enumerate(TERMS):
                            last = pe.matmul(y_ps[:, dt, 0:T], w2[:, slot, a, k, dt * P:(dt + 1) * P],
                                             hid_hl[:, slot, d, k, :], start=(c == 0 and k == 0 and t == 0),
                                             stop=(c == C - 1 and k == 1 and t == 2))
                last.then_inc(s_y_chunk, 1)

            def turn(e, tt):
                if tt == 0:
                    pe.wait_ge(s_yT, KT * (e + 1))
                if tt >= 2:
                    pe.wait_ge(s_out, 4 * e + tt - 1)
                for dt in range(KT):
                    last = pe.transpose(turn_ps[0:TT, tt % 2, dt * P:(dt + 1) * P], yT[:, dt, tt * TT:(tt + 1) * TT], ident[:])
                last.then_inc(s_turned, 1)

            def body(e, last_out):
                for c in range(C + 1):
                    for k in range(2):
                        if c < C:
                            hidden(e, c, k)
                        if last_out and 1 <= 2 * c + k <= 4:
                            turn(e - 1, 2 * c + k - 1)
                    if c > 0:
                        y(e, c - 1)

            pe.wait_ge(s_ident, 2)
            experts(pe, body)
            for tt in range(4):
                turn(E - 1, tt)

        @block.scalar
        def _(act):
            def xt_hi(e):
                act.wait_ge(s_xt_in, 16 * NB * (e + 1))
                at(act, s_hid_full, 2 * C * e)
                nc.scalar.copy(xt[:, HI].rearrange("p t b l -> p (t b l)"), xt_raw[:].rearrange("p t b l -> p (t b l)")
                               ).then_inc(s_xt_hi, 1)

            def w_hi(e, m, c):
                slot = c % 2
                act.wait_ge(s_w_in[m, slot], 16 * (C // 2 * e + c // 2 + 1))
                if m == 1:
                    at(act, s_hid_full, 2 * (C * e + c - 1))
                    nc.scalar.copy(w1[:, slot, HI], w1_raw[:, slot]).then_inc(s_w_hi[1], 1)
                else:
                    at(act, s_y_chunk, C * e + c - 1)
                    nc.scalar.copy(w2[:, slot, HI], w2_raw[:, slot]).then_inc(s_w_hi[2], 1)

            def gelu(e, c):
                if c == 0:
                    act.wait_ge(s_b1_in, 16 * (e + 1))
                at(act, s_h_lo, C * e + c)
                for k in range(2):
                    act.wait_ge(s_hid_full, 2 * (C * e + c) + k + 1)
                    nc.scalar.activation(hid[:, k, :], hid_ps[:, k, 0:T], ACT.Gelu_apprx_tanh,
                                         bias=b1[:, 2 * c + k:2 * c + k + 1]).then_inc(s_gelu, 1)

            act.wait_ge(s_g_in, 16)
            nc.scalar.activation(gate[:], g_in[:], ACT.Tanh).then_inc(s_gate, 1)

            def body(e, _):
                xt_hi(e)
                w_hi(e, 1, 0)
                for c in range(C):
                    if c + 1 < C:
                        w_hi(e, 1, c + 1)
                    w_hi(e, 2, c)
                    gelu(e, c)

            experts(act, body)

        @block.vector
        def _(dve):
            def xt_lo(e):
                dve.wait_ge(s_xt_hi, e + 1)
                nc.vector.tensor_tensor(xt[:, LO].rearrange("p t b l -> p (t b l)"), xt_raw[:].rearrange("p t b l -> p (t b l)"),
                                        xt[:, HI].bitcast(F32).rearrange("p t b l -> p (t b l)"), ALU.subtract
                                        ).then_inc(s_xt_lo, 1)

            def w_lo(e, m, c):
                slot = c % 2
                w, raw = (w1, w1_raw) if m == 1 else (w2, w2_raw)
                dve.wait_ge(s_w_hi[m], C * e + c + 1)
                nc.vector.tensor_tensor(w[:, slot, LO], raw[:, slot], w[:, slot, HI].bitcast(F32), ALU.subtract
                                        ).then_inc(s_w_lo[m], 1)

            def split_hidden(e, c):
                slot = c % 2
                dve.wait_ge(s_gelu, 2 * (C * e + c + 1))
                at(dve, s_y_chunk, C * e + c - 1)
                nc.vector.tensor_copy(hid_hl[:, slot, HI], hid[:]).then_inc(s_h_hi, 1)
                dve.wait_ge(s_h_hi, C * e + c + 1)
                nc.vector.tensor_tensor(hid_hl[:, slot, LO], hid[:], hid_hl[:, slot, HI].bitcast(F32), ALU.subtract
                                        ).then_inc(s_h_lo, 1)

            def leave_y(e):
                dve.wait_ge(s_y_chunk, C * (e + 1))
                at(dve, s_turned, 4 * e)
                dve.wait_ge(s_b2_in, 16 * (e + 1))
                for dt in range(KT):
                    nc.vector.tensor_scalar(yT[:, dt, :], y_ps[:, dt, 0:T], b2[:, dt:dt + 1], gate[:, 0:1],
                                            ALU.add, ALU.mult).then_inc(s_yT, 1)

            def add(e, tt):
                dve.wait_ge(s_turned, 4 * e + tt + 1)
                if tt == 0:
                    dve.wait_ge(s_res_in, 16 * (e + 1))
                    at(dve, s_stored, 16 * e)
                nc.vector.tensor_tensor(o[:, tt, :], turn_ps[0:TT, tt % 2, :], res[:, tt, :], ALU.add).then_inc(s_out, 1)

            dve.wait_ge(s_gate, 1)

            def body(e, last_out):
                xt_lo(e)
                w_lo(e, 1, 0)
                if last_out:
                    leave_y(e - 1)
                for c in range(C):
                    if c + 1 < C:
                        w_lo(e, 1, c + 1)
                    w_lo(e, 2, c)
                    for tt in ([0], [1, 2], [3])[c] if c < 3 and last_out else []:
                        add(e - 1, tt)
                    split_hidden(e, c)

            experts(dve, body)
            leave_y(E - 1)
            for tt in range(4):
                add(E - 1, tt)


def build(nc, io, out):
    B, L, D = io["x"].shape
    S = io["ctxT"].shape[2]
    scr = {
        "k": nc.dram_tensor("k_scr", (B, 2, D, S), F32).ap(),
        "q": nc.dram_tensor("q_scr", (B, 2, D, L), F32).ap(),
        "v": nc.dram_tensor("v_scr", (B, S, D), F32).ap(),
        "x1": nc.dram_tensor("x1_scr", (B, L, D), F32).ap(),
        "x1nT": nc.dram_tensor("x1nT_scr", (B, D, L), F32).ap(),
    }
    attention(nc, io, scr)
    feed_forward(nc, io, scr, out)


def kernel(x, ctx_1024, g_xattn, g_ffn, L0_xattn_Wq, L0_xattn_Wk, L0_xattn_Wv, L0_xattn_Wo, L0_ffn_w1, L0_ffn_b1,
           L0_ffn_w2, L0_ffn_b2):
    import numpy as np
    import concourse.bacc as bacc
    from concourse import mybir as mb
    from concourse.bass_utils import run_bass_kernel_spmd

    E, F = L0_ffn_b1.shape
    D = L0_ffn_b2.shape[1]
    laid = {
        "x": x,
        "ctxT": np.asarray(ctx_1024).transpose(0, 2, 1),
        "g_xattn": g_xattn,
        "g_ffn": g_ffn,
        "WQT": np.asarray(L0_xattn_Wq).T,
        "WKT": np.asarray(L0_xattn_Wk).T,
        "WVT": np.asarray(L0_xattn_Wv).T,
        "WOT": np.asarray(L0_xattn_Wo).T,
        "w1": L0_ffn_w1,
        "b1": np.asarray(L0_ffn_b1).reshape(E, F // 128, 128).transpose(0, 2, 1),
        "w2": L0_ffn_w2,
        "b2": np.asarray(L0_ffn_b2).reshape(E, D // 128, 128).transpose(0, 2, 1),
    }
    nc = bacc.Bacc("TRN2", target_bir_lowering=False, num_devices=1)
    arrays, io = {}, {}
    for name, a in laid.items():
        a = np.ascontiguousarray(np.asarray(a))
        arrays[f"{name}_in"] = a
        io[name] = nc.dram_tensor(f"{name}_in", a.shape, mb.dt.from_np(a.dtype), kind="ExternalInput").ap()
    out = nc.dram_tensor("out", x.shape, mb.dt.from_np(np.asarray(x).dtype), kind="ExternalOutput").ap()
    build(nc, io, out)
    r = run_bass_kernel_spmd(nc, [arrays], core_ids=[0])
    return r.results[0]["out"]
```

```python
from contextlib import ExitStack

import concourse.bass as bass
from concourse import mybir

F32 = mybir.dt.float32
F32R = mybir.dt.float32r
I32 = mybir.dt.int32
ALU = mybir.AluOpType
ACT = mybir.ActivationFunctionType

P = 128
HI, LO = 0, 1
TERMS = ((HI, HI), (HI, LO), (LO, HI))
RSQRT_SEED = float(0x5F3759DF)
EPS = 1e-5


def rsqrt_steps(nc, y, v, tmp, var):
    yield lambda: nc.vector.tensor_scalar(v, var, EPS, None, ALU.add)
    yield lambda: nc.vector.tensor_scalar(y.bitcast(I32), v.bitcast(I32), -0.5, RSQRT_SEED, ALU.mult, ALU.add)
    for _ in range(3):
        yield lambda: nc.vector.scalar_tensor_tensor(out=tmp, in0=y, scalar=-0.5, in1=y, op0=ALU.mult, op1=ALU.mult)
        yield lambda: nc.vector.tensor_tensor(tmp, tmp, v, ALU.mult)
        yield lambda: nc.vector.scalar_tensor_tensor(out=y, in0=tmp, scalar=1.5, in1=y, op0=ALU.add, op1=ALU.mult)


LN_STEPS = 2 + 2 + 11


def flamingo_block(nc, io, scr, out):
    B, L, D = io["x"].shape
    S = io["ctxT"].shape[2]
    KT = D // P
    HEADS = 4
    HD = P // HEADS
    LT = L // 2
    SC = S // 3
    ST = S // 6
    STEPS = KT * 3
    SCALE = float(HD) ** -0.5
    E, _, F = io["w1"].shape
    T = B * L // E
    TT = T // 4
    FC = 2 * P
    C = F // FC
    NB = T // L
    assert L == 2 * LT and S == 6 * ST and LT <= P and ST <= P and 2 * L <= 512
    assert T == NB * L and TT == LT and T <= 512 and C % 2 == 0 and C >= 4 and E >= 3 and B >= 6

    PREP, OUT = "TKVQ", "OU"
    FILL = [(0, "A", "T", 0), (0, "A", "T", 1), (0, "B", "K", 0),
            (1, "A", "K", 1), (1, "B", "O", 0), (2, "A", "K", 2), (2, "B", "O", 1),
            (3, "A", "K", 3), (3, "B", "V", 0), (4, "A", "K", 4), (4, "B", "V", 1),
            (5, "A", "K", 5), (5, "B", "Q", 0), (5, "B", "U", 0), (5, "B", "U", 1),
            (6, "A", "K", 6), (6, "B", "V", 2), (7, "A", "K", 7), (7, "B", "V", 3),
            (8, "A", "K", 8), (8, "B", "Q", 1), (8, "B", "Q", 2),
            (9, "A", "K", 9), (9, "B", "V", 4), (10, "A", "K", 10), (10, "B", "V", 5),
            (11, "A", "K", 11), (11, "B", "Q", 3)]
    FILL_FIRST = [(4, "B", "T", 0), (4, "B", "T", 1)]
    BANK = {(k, i): g % 3 for g, (_, _, k, i) in enumerate(FILL)}
    BANK["T", 0], BANK["T", 1] = 1, 0
    COUNT = {"T": 2, "K": 12, "V": 6, "Q": 4, "O": 2, "U": 2}

    def known(b, value):
        return isinstance(b, int) and b == value

    def fill_of(b, prep, out_):
        if known(b, -1):
            order = sorted([f for f in FILL if f[2] != "T"] + FILL_FIRST, key=lambda f: f[0:2])
        else:
            order = FILL
        return [(s, a, k, i) for s, a, k, i in order if (k in PREP and prep) or (k in OUT and out_)]

    def fill_at(b, prep, out_, s, side):
        return [(k, i) for t, a, k, i in fill_of(b, prep, out_) if (t, a) == (s, side)]

    def attends(b):
        return not isinstance(b, int) or 0 <= b < B

    def follows(b):
        return not isinstance(b, int) or b > 0

    def nth(kind, b, i):
        return COUNT[kind] * (b + 1 if kind in PREP else b - 1) + i + 1

    def own(eng):
        eng.nop(nofuse=True)

    def at(eng, sem_, value):
        if not isinstance(value, int) or value > 0:
            eng.wait_ge(sem_, value)

    def alone(eng, sem_, value):
        at(eng, sem_, value)
        own(eng)

    def batches(eng, body):
        body(-1, True, False, True)
        body(0, True, False, True)
        body(1, True, True, True)
        with eng.Fori(2, B - 2) as b:
            body(b, True, True, True)
        body(B - 2, True, True, False)
        body(B - 1, False, True, False)
        body(B, False, True, False)

    def experts(eng, body):
        body(0)
        body(1)
        with eng.Fori(2, E) as e:
            body(e)

    with ExitStack() as ctx:
        def sb(name, shape, dt=F32):
            return ctx.enter_context(nc.sbuf_tensor(name, shape, dt))

        def sem(name):
            return ctx.enter_context(nc.semaphore(name))

        scores_ps = ctx.enter_context(nc.psum_tensor("scores_ps", [P, HEADS, 512], F32))
        heads_ps = ctx.enter_context(nc.psum_tensor("heads_ps", [P, 512], F32))
        fill_ps = ctx.enter_context(nc.psum_tensor("fill_ps", [P, 3, 512], F32))

        w = {k: sb(f"w{k}", [P, 2, KT, D], F32R) for k in "KQVO"}
        ctx_raw = sb("ctx_raw", [P, KT, SC])
        ctx_hl = sb("ctx_hl", [P, 3, 2, KT, SC], F32R)
        k_stage = sb("k_stage", [P, 2, 2, SC], F32R)
        q_stage = sb("q_stage", [P, 2, 2, L], F32R)
        v_stage = sb("v_stage", [P, 2, D])
        k_st3 = sb("k_st3", [3 * HD, 2, HEADS, S], F32R)
        q_st3 = sb("q_st3", [3 * HD, 2, HEADS, L], F32R)
        v_sb = sb("v_sb", [ST, 2, 6, P])
        probs = sb("probs", [P, 2, HEADS, 2 * L])
        x_ln = sb("x_ln", [P, 2, D])
        x_res = sb("x_res", [LT, 2, D])
        x1_pair = sb("x1_pair", [LT, 2, 2, D])
        x1, x1n = x1_pair[:, 0], x1_pair[:, 1]
        xnT = sb("xnT", [P, 2, KT, L], F32R)
        oT = sb("oT", [P, 2, KT, L], F32R)
        x1nT = sb("x1nT", [P, KT, L])
        ident = sb("ident", [P, P])
        g_in = sb("g_in", [P, 2])
        gate = sb("gate", [P, 2])
        stats = sb("stats", [LT, 2, 2, 6])
        mv = sb("mv", [LT, 2, 2, 2])
        rstd = sb("rstd", [LT, 2, 2])
        nv = sb("nv", [LT, 2, 2])
        ntmp = sb("ntmp", [LT, 2, 2])
        w1_raw = sb("w1_raw", [P, 2, KT, FC])
        w2_raw = sb("w2_raw", [P, 2, 2, D])
        b1 = sb("b1_sb", [P, 2 * C])
        b2 = sb("b2_sb", [P, KT])

        w_raw = probs[:, :, :, :].rearrange("p a h l -> p (a h l)")
        WR = 3
        HALF = (KT // 2) * D

        w1 = w["K"][:].rearrange("p a t d -> p (a t d)").rearrange("p (s a t f) -> p s a t f", s=2, a=2, t=KT)
        w2 = w["V"][:].rearrange("p a t d -> p (a t d)").rearrange("p (s a t d) -> p s a t d", s=2, a=2, t=2)
        xt = w["Q"][:].rearrange("p a t d -> p (a t d)")[:, 0:2 * KT * T].rearrange("p (a t l) -> p a t l", a=2, t=KT)
        xt_raw = [ctx_raw[:].rearrange("p t s -> p (t s)")[:, 0:2 * T].rearrange("p (t l) -> p t l", t=2),
                  v_stage[:].rearrange("p a d -> p (a d)")[:, 0:2 * T].rearrange("p (t l) -> p t l", t=2)]
        hid = x_ln[:].rearrange("p t d -> p (t d)")[:, 0:2 * T].rearrange("p (k l) -> p k l", k=2)
        hid_hl = ctx_hl[:].rearrange("p c a t s -> p (c a t s)")[:, 0:8 * T].rearrange("p (s a k l) -> p s a k l", s=2, a=2, k=2)
        yT = w_raw[:, 0:KT * T].rearrange("p (t l) -> p t l", t=KT)
        res = x1_pair[:].rearrange("p a t d -> p (a t) d")
        y_ps = scores_ps
        hid_ps = [heads_ps[:], fill_ps[:, 0, :]]
        turn_ps = [fill_ps[:, 1, :], fill_ps[:, 2, :]]

        s_w_in = [sem(f"w_in{r}") for r in range(WR)]
        s_w_hi, s_w_lo = sem("w_hi"), sem("w_lo")
        s_ctx_in, s_ctx_hi, s_ctx_lo = sem("ctx_in"), sem("ctx_hi_s"), sem("ctx_lo_s")
        s_x_in, s_xr_in, s_g_in, s_gate = sem("x_in"), sem("xr_in"), sem("g_in_s"), sem("gate_s")
        s_ident = sem("ident_s")
        s_xn = sem("xn_ready")
        s_x1, s_x1n = sem("x1_ready"), sem("x1n_ready")
        s_ln = [sem("ln_x_step"), sem("ln_x1_step")]
        full = {k: sem(f"full_{k}") for k in "TKVQOU"}
        hi = {k: sem(f"hi_{k}") for k in "TKQ"}
        done = {k: sem(f"done_{k}") for k in "TKVQU"}
        done["O"] = s_x1
        s_kq_in = [sem(f"kq_in{r}") for r in range(2)]
        s_v_in = [sem(f"v_in{r}") for r in range(2)]
        s_scores, s_probs, s_av = sem("scores_full"), sem("probs_ready"), sem("av_done")
        s_o_hi, s_o_lo = sem("oT_hi"), sem("oT_lo")
        s_k_st = [sem(f"k_stored{r}") for r in range(2)]
        s_q_st = [sem(f"q_stored{r}") for r in range(2)]
        s_v_st = [sem(f"v_stored{r}") for r in range(2)]
        s_x1_st, s_x1nT_st = sem("x1_stored"), sem("x1nT_stored")
        s_ew_in = {(m, r): sem(f"w{m}_in{r}") for m in (1, 2) for r in range(2)}
        s_ew_hi = {m: sem(f"w{m}_hi") for m in (1, 2)}
        s_ew_lo = {m: sem(f"w{m}_lo") for m in (1, 2)}
        s_xt_in, s_xt_hi, s_xt_lo = sem("xt_in"), sem("xt_hi"), sem("xt_lo")
        s_b1_in, s_b2_in, s_res_in = sem("b1_in"), sem("b2_in"), sem("res_in")
        s_hid_full, s_gelu, s_h_hi, s_h_lo = sem("hid_full"), sem("gelu_ready"), sem("hid_hi"), sem("hid_lo")
        s_y_chunk, s_yT, s_turned, s_out, s_stored = sem("y_chunk"), sem("yT_ready"), sem("turned"), sem("out_ready"), sem("out_stored")

        block = ctx.enter_context(nc.Block())

        @block.sync
        def _(sp):
            def load_ctx(n, c):
                alone(sp, s_ctx_lo, 3 * n + c)
                sp.dma_start(ctx_raw[:], io["ctxT"][bass.ds(n, 1), :, c * SC:(c + 1) * SC]
                             .rearrange("a (t p) s -> p (a t) s", p=P)).then_inc(s_ctx_in, 16)

            def load_x(dst, b, s):
                sp.dma_start(dst, io["x"][bass.ds(b, 1)].rearrange("a (t p) d -> p (a t) d", p=LT)).then_inc(s, 16)

            def load_kq(b, mt, kq_b):
                slot = mt % 2
                alone(sp, s_scores, STEPS * kq_b + 3 * ((mt - 2) % KT) + 3)
                alone(sp, s_k_st[slot], 16 * (6 * b + (8 + mt) // 2 + 1))
                alone(sp, s_q_st[slot], 16 * (2 * b + mt // 2 + 1))
                for t, (kh, qh) in enumerate(((HI, HI), (LO, HI), (HI, LO))):
                    for dst, src, h in ((k_st3, scr["k"], kh), (q_st3, scr["q"], qh)):
                        sp.dma_start(dst[t * HD:(t + 1) * HD, slot].bitcast(F32),
                                     src[bass.ds(b, 1), h, mt * P:(mt + 1) * P, :]
                                     .rearrange("a (j p) s -> p (a j) s", p=HD)).then_inc(s_kq_in[slot], 16)

            def load_v(b, mt, v_b):
                slot = mt % 2
                alone(sp, s_av, STEPS * v_b + 3 * ((mt - 2) % KT) + 3)
                for r in range(2):
                    alone(sp, s_v_st[r], 16 * 3 * (b + 1))
                sp.dma_start(v_sb[:, slot], scr["v"][bass.ds(b, 1), :, mt * P:(mt + 1) * P]
                             .rearrange("a (t p) d -> p (a t) d", p=ST)).then_inc(s_v_in[slot], 16)

            def load_w(n):
                kind, half = "KVQO"[n // 2], n % 2
                r = n % WR
                at(sp, s_w_lo, n - WR + 1)
                sp.dma_start(w_raw[:, r * HALF:(r + 1) * HALF].rearrange("p (t d) -> p t d", d=D),
                             io[f"W{kind}T"].rearrange("(t p) d -> p t d", p=P)[:, half * KT // 2:(half + 1) * KT // 2]
                             ).then_inc(s_w_in[r], 16)

            def body(b, prep, out_, ahead):
                here = attends(b)
                if prep:
                    load_ctx(b + 1, 1)
                if here:
                    load_v(b, 1, b - 1)
                if known(b, -1):
                    for n in range(6, 8):
                        load_w(n)
                if prep:
                    load_ctx(b + 1, 2)
                if here:
                    load_kq(b, 2, b)
                    alone(sp, s_x1, 2 * b)
                    load_x(x_res[:], b, s_xr_in)
                if ahead:
                    alone(sp, full["T"], nth("T", b, 1))
                    load_x(x_ln[0:LT], b + 2, s_x_in)
                if here:
                    load_v(b, 2, b)
                if ahead:
                    load_ctx(b + 2, 0)
                if here:
                    load_kq(b, 3, b)
                    load_v(b, 3, b)
                if prep:
                    load_kq(b + 1, 0, b)
                    load_v(b + 1, 0, b)
                    load_kq(b + 1, 1, b)
                if known(b, B - 1):
                    expert_start()

            def load_xt(e):
                if known(e, 0):
                    alone(sp, s_ctx_lo, 3 * B)
                    for r in range(2):
                        alone(sp, s_v_st[r], 16 * 3 * B)
                    alone(sp, s_x1nT_st, 16 * NB)
                alone(sp, s_xt_lo, 2 * e)
                if known(e, 1):
                    alone(sp, s_x1nT_st, 16 * B)
                    alone(sp, s_x1_st, 16 * B)
                for half in range(2):
                    for i in range(NB):
                        sp.dma_start(xt_raw[half][:, :, i * L:(i + 1) * L],
                                     scr["x1nT"][bass.ds(e * NB + i, 1), half * D // 2:(half + 1) * D // 2, :]
                                     .rearrange("b (t p) l -> p (b t) l", p=P)).then_inc(s_xt_in, 16)

            def load_w1(e, c):
                alone(sp, s_ew_lo[1], C * e + c - 1)
                sp.dma_start(w1_raw[:, c % 2], io["w1"][bass.ds(e, 1), :, c * FC:(c + 1) * FC]
                             .rearrange("a (t p) f -> p (a t) f", p=P)).then_inc(s_ew_in[1, c % 2], 16)

            def load_w2(e, c):
                alone(sp, s_ew_lo[2], C * e + c - 1)
                sp.dma_start(w2_raw[:, c % 2], io["w2"][bass.ds(e, 1), c * FC:(c + 1) * FC, :]
                             .rearrange("a (t p) d -> p (a t) d", p=P)).then_inc(s_ew_in[2, c % 2], 16)

            def load_b1(e):
                alone(sp, s_gelu, 2 * C * e)
                sp.dma_start(b1[:], io["b1"][bass.ds(e, 1)].rearrange("a p f -> p (a f)")).then_inc(s_b1_in, 16)

            def expert_start():
                load_w1(0, 0)
                load_w2(0, 0)
                load_w1(0, 1)
                load_xt(0)
                load_b1(0)

            def expert(e):
                if not known(e, 0):
                    load_xt(e)
                for c in range(C):
                    if not (known(e, 0) and c < 2):
                        load_w1(e, c)
                    if c == 0 and not known(e, 0):
                        load_b1(e)
                    if not (known(e, 0) and c < 1):
                        load_w2(e, c)
                    if c == 2:
                        alone(sp, s_yT, KT * e)
                        sp.dma_start(b2[:], io["b2"][bass.ds(e, 1)].rearrange("a p f -> p (a f)")).then_inc(s_b2_in, 16)
                    if c == 5:
                        if known(e, 0):
                            alone(sp, s_x1_st, 16 * B)
                            alone(sp, full["U"], 2 * B)
                        alone(sp, s_stored, 16 * e)
                        sp.dma_start(res, scr["x1"][bass.ds(e * NB, NB)].rearrange("b (t p) d -> p (b t) d", p=TT)
                                     ).then_inc(s_res_in, 16)

            load_w(0)
            load_ctx(0, 0)
            load_w(1)
            load_w(2)
            load_x(x_ln[0:LT], 0, s_x_in)
            sp.dma_start(g_in[:, 0:1], io["g_xattn"].partition_broadcast(P)).then_inc(s_g_in, 16)
            sp.dma_start(g_in[:, 1:2], io["g_ffn"].partition_broadcast(P)).then_inc(s_g_in, 16)
            for n in range(3, 6):
                load_w(n)
            batches(sp, body)
            experts(sp, expert)

        @block.gpsimd
        def _(pool):
            nc.gpsimd.memset(ident[:], 0.0).then_inc(s_ident, 1)
            pool.wait_ge(s_ident, 1)
            nc.gpsimd.affine_select(out=ident[:], in_=ident[:], compare_op=ALU.not_equal, fill=1.0, base=0,
                                    pattern=[[-1, P]], channel_multiplier=1).then_inc(s_ident, 1)

            def body(b, prep, out_, ahead):
                n = b + 1
                for _, _, kind, i in fill_of(b, prep, out_):
                    if kind in "KVQ":
                        alone(pool, done[kind], nth(kind, b, i))
                    if kind == "K":
                        c, mt = i // KT, i % KT
                        pool.dma_start(scr["k"][bass.ds(n, 1), :, mt * P:(mt + 1) * P, c * SC:(c + 1) * SC]
                                       .rearrange("a h p s -> p (a h) s"), k_stage[:, i % 2].bitcast(F32)
                                       ).then_inc(s_k_st[i % 2], 16)
                    if kind == "Q":
                        pool.dma_start(scr["q"][bass.ds(n, 1), :, i * P:(i + 1) * P, :]
                                       .rearrange("a h p s -> p (a h) s"), q_stage[:, i % 2].bitcast(F32)
                                       ).then_inc(s_q_st[i % 2], 16)
                    if kind == "V":
                        pool.dma_start(scr["v"][bass.ds(n, 1), i * ST:(i + 1) * ST, :]
                                       .rearrange("a p d -> p (a d)"), v_stage[0:ST, i % 2]).then_inc(s_v_st[i % 2], 16)
                    if (kind, i) == ("O", 1):
                        alone(pool, s_x1, 2 * b)
                        pool.dma_start(scr["x1"][bass.ds(b - 1, 1)].rearrange("a (t p) d -> p (a t) d", p=LT),
                                       x1).then_inc(s_x1_st, 16)
                    if (kind, i) == ("U", 1):
                        alone(pool, done["U"], 2 * b)
                        pool.dma_start(scr["x1nT"][bass.ds(b - 1, 1)].rearrange("a (t p) l -> p (a t) l", p=P),
                                       x1nT[:]).then_inc(s_x1nT_st, 16)

            batches(pool, body)

            with pool.Fori(0, E) as e:
                alone(pool, s_out, 4 * e + 4)
                pool.dma_start(out[bass.ds(e * NB, NB)].rearrange("b (t p) d -> p (b t) d", p=TT), res
                               ).then_inc(s_stored, 16)
            pool.wait_ge(s_x1_st, 16 * B)
            pool.wait_ge(s_x1nT_st, 16 * B)
            for r in range(2):
                pool.wait_ge(s_k_st[r], 16 * 6 * B)
                pool.wait_ge(s_q_st[r], 16 * 2 * B)
                pool.wait_ge(s_v_st[r], 16 * 3 * B)
            pool.wait_ge(s_stored, 16 * E)

        @block.tensor
        def _(pe):
            def three_terms(out_, lhsT, rhs):
                for kt in range(KT):
                    for t, (a, c) in enumerate(TERMS):
                        last = pe.matmul(out_, lhsT(kt, a), rhs(kt, c), start=(kt == 0 and t == 0),
                                         stop=(kt == KT - 1 and t == 2))
                return last

            def bank_free(b, prep, out_, kind, i):
                todo = [(k, j) for _, _, k, j in fill_of(b, prep, out_)]
                mine = todo.index((kind, i))
                before = [g for g in todo[:mine] if BANK[g] == BANK[kind, i]]
                if before:
                    k, j = before[-1]
                    pe.wait_ge(done[k], nth(k, b, j))
                    return
                if known(b, -1):
                    return
                last = fill_of(b - 1, not known(b, B), not (known(b, 0) or known(b, 1)))
                k, j = [(k, j) for _, _, k, j in last if BANK[k, j] == BANK[kind, i]][-1]
                pe.wait_ge(done[k], nth(k, b - 1, j))

            def scores(b, s):
                mt, pair = s // 3, s % 3
                slot = mt % 2
                if pair == 0:
                    pe.wait_ge(s_kq_in[slot], 16 * 6 * (2 * b + mt // 2 + 1))
                at(pe, s_probs, STEPS * b + s)
                for t in range(2):
                    for j in range(HEADS):
                        st = 2 * pair + t
                        last = pe.matmul(scores_ps[0:ST, j, t * L:(t + 1) * L],
                                         k_st3[:, slot, j, st * ST:(st + 1) * ST], q_st3[:, slot, j, :],
                                         start=True, stop=True)
                last.then_inc(s_scores, 1)

            def heads(b, s):
                mt, pair = s // 3, s % 3
                slot = mt % 2
                if pair == 0:
                    pe.wait_ge(s_v_in[slot], 16 * (2 * b + mt // 2 + 1))
                    at(pe, s_o_lo, KT * b + mt)
                pe.wait_ge(s_probs, STEPS * b + s + 1)
                for t in range(2):
                    for j in range(HEADS):
                        last = pe.matmul(heads_ps[j * HD:(j + 1) * HD, 0:L],
                                         v_sb[:, slot, 2 * pair + t, j * HD:(j + 1) * HD],
                                         probs[0:ST, s % 2, j, t * L:(t + 1) * L],
                                         start=(pair == 0 and t == 0), stop=(pair == 2 and t == 1))
                last.then_inc(s_av, 1)

            def fill(b, prep, out_, kind, i):
                bank_free(b, prep, out_, kind, i)
                ps = fill_ps[:, BANK[kind, i], :]
                n = b + 1
                if kind == "T":
                    if i == 0:
                        pe.wait_ge(s_xn, n + 1)
                    for kt in range(KT):
                        last = pe.transpose(ps[:, kt * LT:(kt + 1) * LT], x_ln[0:LT, i, kt * P:(kt + 1) * P], ident[0:LT, 0:LT])
                elif kind == "K":
                    c, mt = i // KT, i % KT
                    if mt == 0:
                        pe.wait_ge(s_ctx_lo, 3 * n + c + 1)
                    if known(n, 0) and i == 0:
                        pe.wait_ge(s_w_lo, 2)
                    last = three_terms(ps[:, 0:SC], lambda kt, a: w["K"][:, a, kt, mt * P:(mt + 1) * P],
                                       lambda kt, a: ctx_hl[:, c, a, kt, :])
                elif kind == "V":
                    c, r = i // 2, i % 2
                    if known(n, 0) and i == 0:
                        pe.wait_ge(s_w_lo, 4)
                    last = three_terms(ps[0:ST, :], lambda kt, a: ctx_hl[:, c, a, kt, r * ST:(r + 1) * ST],
                                       lambda kt, a: w["V"][:, a, kt, :])
                elif kind == "Q":
                    if i == 0:
                        pe.wait_ge(done["T"], nth("T", b, 1))
                    if known(n, 0) and i == 0:
                        pe.wait_ge(s_w_lo, 6)
                    last = three_terms(ps[:, 0:L], lambda kt, a: w["Q"][:, a, kt, i * P:(i + 1) * P],
                                       lambda kt, a: xnT[:, a, kt, :])
                elif kind == "O":
                    if i == 0:
                        pe.wait_ge(s_o_lo, KT * b)
                        if known(b, 1):
                            pe.wait_ge(s_w_lo, 8)
                    last = three_terms(ps[0:LT, :], lambda kt, a: oT[:, a, kt, i * LT:(i + 1) * LT],
                                       lambda kt, a: w["O"][:, a, kt, :])
                else:
                    if i == 0:
                        pe.wait_ge(s_x1n, b)
                    for kt in range(KT):
                        last = pe.transpose(ps[:, kt * LT:(kt + 1) * LT], x1n[:, i, kt * P:(kt + 1) * P], ident[0:LT, 0:LT])
                last.then_inc(full[kind], 1)

            def body(b, prep, out_, ahead):
                for s in range(STEPS):
                    if attends(b):
                        scores(b, s)
                    for kind, i in fill_at(b, prep, out_, s, "A"):
                        fill(b, prep, out_, kind, i)
                    if s == 0 and follows(b):
                        heads(b - 1, STEPS - 1)
                    if s > 0 and attends(b):
                        heads(b, s - 1)
                    for kind, i in fill_at(b, prep, out_, s, "B"):
                        if known(b, B) and (kind, i) == ("U", 0):
                            for k in range(2):
                                hidden(0, 0, k)
                        fill(b, prep, out_, kind, i)

            def hidden(e, c, k):
                slot = c % 2
                if k == 0:
                    pe.wait_ge(s_ew_lo[1], C * e + c + 1)
                    if c == 0:
                        pe.wait_ge(s_xt_lo, 2 * (e + 1))
                if known(e, 0) and c == 0:
                    if k == 0:
                        pe.wait_ge(s_o_lo, KT * B)
                    else:
                        pe.wait_ge(s_x1, 2 * B)
                at(pe, s_gelu, 2 * (C * e + c - 1) + k + 1)
                for kt in range(KT):
                    for t, (a, d) in enumerate(TERMS):
                        last = pe.matmul(hid_ps[k][:, 0:T], w1[:, slot, a, kt, k * P:(k + 1) * P], xt[:, d, kt, :],
                                         start=(kt == 0 and t == 0), stop=(kt == KT - 1 and t == 2))
                last.then_inc(s_hid_full, 1)

            def y(e, c):
                slot = c % 2
                pe.wait_ge(s_ew_lo[2], C * e + c + 1)
                pe.wait_ge(s_h_lo, C * e + c + 1)
                if c == 0:
                    at(pe, s_yT, KT * e)
                for dt in range(KT):
                    for k in range(2):
                        for t, (a, d) in enumerate(TERMS):
                            last = pe.matmul(y_ps[:, dt, 0:T], w2[:, slot, a, k, dt * P:(dt + 1) * P],
                                             hid_hl[:, slot, d, k, :], start=(c == 0 and k == 0 and t == 0),
                                             stop=(c == C - 1 and k == 1 and t == 2))
                last.then_inc(s_y_chunk, 1)

            def turn(e, tt):
                if tt == 0:
                    pe.wait_ge(s_yT, KT * (e + 1))
                    if known(e, 0):
                        pe.wait_ge(done["U"], 2 * B)
                if tt >= 2:
                    pe.wait_ge(s_out, 4 * e + tt - 1)
                for dt in range(KT):
                    last = pe.transpose(turn_ps[tt % 2][0:TT, dt * P:(dt + 1) * P], yT[:, dt, tt * TT:(tt + 1) * TT], ident[:])
                last.then_inc(s_turned, 1)

            def expert(e):
                for c in range(C + 1):
                    for k in range(2):
                        if c < C and not (known(e, 0) and c == 0):
                            hidden(e, c, k)
                        if not known(e, 0) and 1 <= 2 * c + k <= 4:
                            turn(e - 1, 2 * c + k - 1)
                    if c > 0:
                        y(e, c - 1)

            pe.wait_ge(s_ident, 2)
            batches(pe, body)
            experts(pe, expert)
            for tt in range(4):
                turn(E - 1, tt)

        def split_points(s):
            return {1: (1, 1), 4: (1, 2), 8: (2, 0)}.get(s)

        W_SPLITS = {0: (2, 3), 2: (4,), 3: (5,), 6: (6,), 7: (7,)}

        @block.scalar
        def _(act):
            def ctx_hi(n, c):
                act.wait_ge(s_ctx_in, 16 * (3 * n + c + 1))
                at(act, full["K"], 12 * (n - 1) + KT * (c + 1))
                at(act, full["V"], 6 * (n - 1) + 2 * (c + 1))
                nc.scalar.copy(ctx_hl[:, c, HI], ctx_raw[:]).then_inc(s_ctx_hi, 1)

            def w_hi(n):
                act.wait_ge(s_w_in[n % WR], 16 * (n // WR + 1))
                nc.scalar.copy(w["KVQO"[n // 2]][:, HI, (n % 2) * KT // 2:(n % 2 + 1) * KT // 2, :],
                               w_raw[:, (n % WR) * HALF:(n % WR + 1) * HALF].rearrange("p (t d) -> p t d", d=D)
                               ).then_inc(s_w_hi, 1)

            def sigmoid(b, s):
                act.wait_ge(s_scores, STEPS * b + s + 1)
                at(act, s_av, STEPS * b + s - 1)
                if known(b, 0) and s == 0:
                    act.wait_ge(s_w_lo, 8)
                nc.scalar.activation(probs[0:ST, s % 2], scores_ps[0:ST, :, 0:2 * L], ACT.Sigmoid,
                                     scale=SCALE).then_inc(s_probs, 1)

            def o_hi(b, mt):
                act.wait_ge(s_av, STEPS * b + 3 * mt + 3)
                if mt == 0:
                    at(act, full["O"], 2 * b)
                nc.scalar.copy(oT[:, HI, mt, :], heads_ps[:, 0:L]).then_inc(s_o_hi, 1)

            def leave(b, kind, i):
                n = b + 1
                if kind == "O":
                    return
                act.wait_ge(full[kind], nth(kind, b, i))
                ps = fill_ps[:, BANK[kind, i], :]
                if kind == "T":
                    if i == 0:
                        at(act, full["Q"], 4 * n)
                    nc.scalar.copy(xnT[:, HI, :, i * LT:(i + 1) * LT],
                                   ps[:, 0:KT * LT].rearrange("p (t l) -> p t l", l=LT)).then_inc(hi["T"], 1)
                elif kind == "K":
                    at(act, s_k_st[i % 2], 16 * (6 * n + i // 2))
                    nc.scalar.copy(k_stage[:, i % 2, HI, :], ps[:, 0:SC]).then_inc(hi["K"], 1)
                elif kind == "Q":
                    at(act, s_q_st[i % 2], 16 * (2 * n + i // 2))
                    nc.scalar.copy(q_stage[:, i % 2, HI, :], ps[:, 0:L]).then_inc(hi["Q"], 1)
                elif kind == "V":
                    at(act, s_v_st[i % 2], 16 * (3 * n + i // 2))
                    nc.scalar.copy(v_stage[0:ST, i % 2, :], ps[0:ST, :]).then_inc(done["V"], 1)
                else:
                    if i == 0:
                        at(act, s_x1nT_st, 16 * (b - 1))
                    nc.scalar.copy(x1nT[:, :, i * LT:(i + 1) * LT],
                                   ps[:, 0:KT * LT].rearrange("p (t l) -> p t l", l=LT)).then_inc(done["U"], 1)

            def body(b, prep, out_, ahead):
                for s in range(STEPS):
                    if attends(b):
                        sigmoid(b, s)
                    for kind, i in fill_at(b, prep, out_, s, "A"):
                        leave(b, kind, i)
                    if s == 0 and follows(b):
                        o_hi(b - 1, KT - 1)
                    if s > 0 and s % 3 == 0 and attends(b):
                        o_hi(b, s // 3 - 1)
                    for kind, i in fill_at(b, prep, out_, s, "B"):
                        if known(b, B) and (kind, i) == ("U", 0):
                            gelu(0, 0)
                        leave(b, kind, i)
                    if known(b, -1):
                        for n in W_SPLITS.get(s, ()):
                            w_hi(n)
                    split = split_points(s)
                    if split and (prep if split[0] == 1 else ahead):
                        ctx_hi(b + split[0], split[1])
                    if known(b, B - 1):
                        if s == 7:
                            e_hi(0, 1, 0)
                        if s == 8:
                            e_hi(0, 2, 0)
                        if s == 9:
                            xt_hi(0)
                        if s == 11:
                            e_hi(0, 1, 1)

            def xt_hi(e):
                act.wait_ge(s_xt_in, 16 * 2 * NB * (e + 1))
                at(act, s_hid_full, 2 * C * e)
                if known(e, 0):
                    act.wait_ge(full["Q"], 4 * B)
                for half in range(2):
                    nc.scalar.copy(xt[:, HI, 2 * half:2 * half + 2, :], xt_raw[half]).then_inc(s_xt_hi, 1)

            def e_hi(e, m, c):
                slot = c % 2
                act.wait_ge(s_ew_in[m, slot], 16 * (C // 2 * e + c // 2 + 1))
                if known(e, 0) and c == 0:
                    act.wait_ge(full["K"] if m == 1 else full["V"], (12 if m == 1 else 6) * B)
                if m == 1:
                    at(act, s_hid_full, 2 * (C * e + c - 1))
                    nc.scalar.copy(w1[:, slot, HI], w1_raw[:, slot]).then_inc(s_ew_hi[1], 1)
                else:
                    at(act, s_y_chunk, C * e + c - 1)
                    nc.scalar.copy(w2[:, slot, HI], w2_raw[:, slot]).then_inc(s_ew_hi[2], 1)

            def gelu(e, c):
                if c == 0:
                    act.wait_ge(s_b1_in, 16 * (e + 1))
                    if known(e, 0):
                        act.wait_ge(full["T"], 2 * B)
                at(act, s_h_lo, C * e + c)
                for k in range(2):
                    act.wait_ge(s_hid_full, 2 * (C * e + c) + k + 1)
                    nc.scalar.activation(hid[:, k, :], hid_ps[k][:, 0:T], ACT.Gelu_apprx_tanh,
                                         bias=b1[:, 2 * c + k:2 * c + k + 1]).then_inc(s_gelu, 1)

            def expert(e):
                first = known(e, 0)
                if not first:
                    xt_hi(e)
                    e_hi(e, 1, 0)
                for c in range(C):
                    if c + 1 < C and not (first and c == 0):
                        e_hi(e, 1, c + 1)
                    if not (first and c == 0):
                        e_hi(e, 2, c)
                        gelu(e, c)

            w_hi(0)
            ctx_hi(0, 0)
            w_hi(1)
            act.wait_ge(s_g_in, 32)
            nc.scalar.activation(gate[:], g_in[:], ACT.Tanh).then_inc(s_gate, 1)
            batches(act, body)
            experts(act, expert)

        @block.vector
        def _(dve):
            def ctx_lo(n, c):
                dve.wait_ge(s_ctx_hi, 3 * n + c + 1)
                nc.vector.tensor_tensor(ctx_hl[:, c, LO], ctx_raw[:], ctx_hl[:, c, HI].bitcast(F32),
                                        ALU.subtract).then_inc(s_ctx_lo, 1)

            def w_lo(n):
                dve.wait_ge(s_w_hi, n + 1)
                part = w["KVQO"[n // 2]][:, :, (n % 2) * KT // 2:(n % 2 + 1) * KT // 2, :]
                nc.vector.tensor_tensor(part[:, LO],
                                        w_raw[:, (n % WR) * HALF:(n % WR + 1) * HALF].rearrange("p (t d) -> p t d", d=D),
                                        part[:, HI].bitcast(F32), ALU.subtract).then_inc(s_w_lo, 1)

            def layernorm(which, n, src, dst, ready):
                steps = [lambda t=t: nc.vector.bn_stats(stats[:, which, t, :], src[:, t, :]) for t in range(2)]
                steps += [lambda t=t: nc.vector.bn_aggr(mv[:, which, t, :], stats[:, which, t, :]) for t in range(2)]
                steps += list(rsqrt_steps(nc, rstd[:, which, :], nv[:, which, :], ntmp[:, which, :], mv[:, which, :, 1]))
                for i, step in enumerate(steps):
                    if i in (2, 3):
                        own(dve)
                    step().then_inc(s_ln[which], 1)
                    dve.wait_ge(s_ln[which], LN_STEPS * n + i + 1)
                for t in range(2):
                    last = nc.vector.tensor_scalar(dst[:, t, :], src[:, t, :], mv[:, which, t, 0:1],
                                                   rstd[:, which, t:t + 1], ALU.subtract, ALU.mult)
                last.then_inc(ready, 1)

            def ln_x(n):
                dve.wait_ge(s_x_in, 16 * (n + 1))
                layernorm(0, n, x_ln[0:LT], x_ln[0:LT], s_xn)

            def ln_x1(b):
                dve.wait_ge(s_x1, 2 * b)
                at(dve, full["U"], 2 * (b - 1))
                layernorm(1, b - 1, x1, x1n, s_x1n)

            def o_lo(b, mt):
                dve.wait_ge(s_o_hi, KT * b + mt + 1)
                nc.vector.tensor_tensor(oT[:, LO, mt, :], heads_ps[:, 0:L], oT[:, HI, mt, :].bitcast(F32),
                                        ALU.subtract).then_inc(s_o_lo, 1)

            def leave(b, kind, i):
                ps = fill_ps[:, BANK[kind, i], :]
                if kind in "TKQ":
                    dve.wait_ge(hi[kind], nth(kind, b, i))
                if kind == "T":
                    nc.vector.tensor_tensor(xnT[:, LO, :, i * LT:(i + 1) * LT],
                                            ps[:, 0:KT * LT].rearrange("p (t l) -> p t l", l=LT),
                                            xnT[:, HI, :, i * LT:(i + 1) * LT].bitcast(F32),
                                            ALU.subtract).then_inc(done["T"], 1)
                elif kind == "K":
                    nc.vector.tensor_tensor(k_stage[:, i % 2, LO, :], ps[:, 0:SC], k_stage[:, i % 2, HI, :].bitcast(F32),
                                            ALU.subtract).then_inc(done["K"], 1)
                elif kind == "Q":
                    nc.vector.tensor_tensor(q_stage[:, i % 2, LO, :], ps[:, 0:L], q_stage[:, i % 2, HI, :].bitcast(F32),
                                            ALU.subtract).then_inc(done["Q"], 1)
                elif kind == "O":
                    dve.wait_ge(full["O"], nth("O", b, i))
                    if i == 0:
                        dve.wait_ge(s_xr_in, 16 * b)
                        if known(b, 1):
                            dve.wait_ge(s_gate, 1)
                        at(dve, s_x1_st, 16 * (b - 1))
                    nc.vector.scalar_tensor_tensor(out=x1[:, i, :], in0=ps[0:LT, :], scalar=gate[0:LT, 0:1],
                                                   in1=x_res[:, i, :], op0=ALU.mult, op1=ALU.add).then_inc(s_x1, 1)

            def body(b, prep, out_, ahead):
                for s in range(STEPS):
                    for kind, i in fill_at(b, prep, out_, s, "A"):
                        leave(b, kind, i)
                    if s == 0 and follows(b):
                        o_lo(b - 1, KT - 1)
                    if s > 0 and s % 3 == 0 and attends(b):
                        o_lo(b, s // 3 - 1)
                    for kind, i in fill_at(b, prep, out_, s, "B"):
                        leave(b, kind, i)
                    if known(b, -1):
                        for n in W_SPLITS.get(s, ()):
                            w_lo(n)
                        if s == 2:
                            ln_x(0)
                    split = split_points(s)
                    if split and (prep if split[0] == 1 else ahead):
                        ctx_lo(b + split[0], split[1])
                    if s == 3 and out_:
                        ln_x1(b)
                    if s == 6 and ahead:
                        ln_x(b + 2)
                    if known(b, B - 1):
                        if s == 7:
                            e_lo(0, 1, 0)
                        if s == 8:
                            e_lo(0, 2, 0)
                        if s == 9:
                            xt_lo(0)
                        if s == 11:
                            e_lo(0, 1, 1)
                if known(b, B):
                    split_hidden(0, 0)

            def xt_lo(e):
                for half in range(2):
                    dve.wait_ge(s_xt_hi, 2 * e + half + 1)
                    nc.vector.tensor_tensor(xt[:, LO, 2 * half:2 * half + 2, :], xt_raw[half],
                                            xt[:, HI, 2 * half:2 * half + 2, :].bitcast(F32), ALU.subtract
                                            ).then_inc(s_xt_lo, 1)

            def e_lo(e, m, c):
                slot = c % 2
                wm, raw = (w1, w1_raw) if m == 1 else (w2, w2_raw)
                dve.wait_ge(s_ew_hi[m], C * e + c + 1)
                nc.vector.tensor_tensor(wm[:, slot, LO], raw[:, slot], wm[:, slot, HI].bitcast(F32), ALU.subtract
                                        ).then_inc(s_ew_lo[m], 1)

            def split_hidden(e, c):
                slot = c % 2
                dve.wait_ge(s_gelu, 2 * (C * e + c + 1))
                at(dve, s_y_chunk, C * e + c - 1)
                if known(e, 0) and c == 0:
                    dve.wait_ge(full["K"], 12 * B)
                    dve.wait_ge(full["V"], 6 * B)
                nc.vector.tensor_copy(hid_hl[:, slot, HI], hid).then_inc(s_h_hi, 1)
                dve.wait_ge(s_h_hi, C * e + c + 1)
                nc.vector.tensor_tensor(hid_hl[:, slot, LO], hid, hid_hl[:, slot, HI].bitcast(F32), ALU.subtract
                                        ).then_inc(s_h_lo, 1)

            def leave_y(e):
                dve.wait_ge(s_y_chunk, C * (e + 1))
                at(dve, s_turned, 4 * e)
                if known(e, 0):
                    dve.wait_ge(s_av, STEPS * B)
                dve.wait_ge(s_b2_in, 16 * (e + 1))
                for dt in range(KT):
                    nc.vector.tensor_scalar(yT[:, dt, :], y_ps[:, dt, 0:T], b2[:, dt:dt + 1], gate[:, 1:2],
                                            ALU.add, ALU.mult).then_inc(s_yT, 1)

            def add(e, tt):
                dve.wait_ge(s_turned, 4 * e + tt + 1)
                if tt == 0:
                    dve.wait_ge(s_res_in, 16 * (e + 1))
                nc.vector.tensor_tensor(res[:, tt, :], turn_ps[tt % 2][0:TT, :], res[:, tt, :], ALU.add).then_inc(s_out, 1)

            def expert(e):
                first = known(e, 0)
                if not first:
                    xt_lo(e)
                    e_lo(e, 1, 0)
                    leave_y(e - 1)
                for c in range(C):
                    if c + 1 < C and not (first and c == 0):
                        e_lo(e, 1, c + 1)
                    if not (first and c == 0):
                        e_lo(e, 2, c)
                    for tt in ([0], [1, 2], [3])[c] if c < 3 and not first else []:
                        add(e - 1, tt)
                    if not (first and c == 0):
                        split_hidden(e, c)

            w_lo(0)
            ctx_lo(0, 0)
            w_lo(1)
            batches(dve, body)
            experts(dve, expert)
            leave_y(E - 1)
            for tt in range(4):
                add(E - 1, tt)


def build(nc, io, out):
    B, L, D = io["x"].shape
    S = io["ctxT"].shape[2]
    scr = {
        "k": nc.dram_tensor("k_scr", (B, 2, D, S), F32).ap(),
        "q": nc.dram_tensor("q_scr", (B, 2, D, L), F32).ap(),
        "v": nc.dram_tensor("v_scr", (B, S, D), F32).ap(),
        "x1": nc.dram_tensor("x1_scr", (B, L, D), F32).ap(),
        "x1nT": nc.dram_tensor("x1nT_scr", (B, D, L), F32).ap(),
    }
    flamingo_block(nc, io, scr, out)


def kernel(x, ctx_1024, g_xattn, g_ffn, L0_xattn_Wq, L0_xattn_Wk, L0_xattn_Wv, L0_xattn_Wo, L0_ffn_w1, L0_ffn_b1,
           L0_ffn_w2, L0_ffn_b2):
    import numpy as np
    import concourse.bacc as bacc
    from concourse import mybir as mb
    from concourse.bass_utils import run_bass_kernel_spmd

    E, F = L0_ffn_b1.shape
    D = L0_ffn_b2.shape[1]
    laid = {
        "x": x,
        "ctxT": np.asarray(ctx_1024).transpose(0, 2, 1),
        "g_xattn": g_xattn,
        "g_ffn": g_ffn,
        "WQT": np.asarray(L0_xattn_Wq).T,
        "WKT": np.asarray(L0_xattn_Wk).T,
        "WVT": np.asarray(L0_xattn_Wv).T,
        "WOT": np.asarray(L0_xattn_Wo).T,
        "w1": L0_ffn_w1,
        "b1": np.asarray(L0_ffn_b1).reshape(E, F // 128, 128).transpose(0, 2, 1),
        "w2": L0_ffn_w2,
        "b2": np.asarray(L0_ffn_b2).reshape(E, D // 128, 128).transpose(0, 2, 1),
    }
    nc = bacc.Bacc("TRN2", target_bir_lowering=False, num_devices=1)
    arrays, io = {}, {}
    for name, a in laid.items():
        a = np.ascontiguousarray(np.asarray(a))
        arrays[f"{name}_in"] = a
        io[name] = nc.dram_tensor(f"{name}_in", a.shape, mb.dt.from_np(a.dtype), kind="ExternalInput").ap()
    out = nc.dram_tensor("out", x.shape, mb.dt.from_np(np.asarray(x).dtype), kind="ExternalOutput").ap()
    build(nc, io, out)
    r = run_bass_kernel_spmd(nc, [arrays], core_ids=[0])
    return r.results[0]["out"]
```
